# Optimizing a Trainium2 kernel written in Bass

```python
import numpy as np
import jax
import jax.numpy as jnp

def _softmax(x, axis=-1):
    return jax.nn.softmax(x, axis=axis)

def _gelu(x):
    return jax.nn.gelu(x, approximate=True)

def _silu(x):
    return jax.nn.silu(x)

def _sigmoid(x):
    return jax.nn.sigmoid(x)

def _layernorm(x, axis=-1, eps=1e-05):
    m = jnp.mean(x, axis=axis, keepdims=True)
    v = jnp.var(x, axis=axis, keepdims=True)
    return (x - m) / jnp.sqrt(v + eps)

def _scatter_add(tgt, idx, src, axis=0):
    return tgt.at[idx].add(src)

def _segment_sum(src, seg, n):
    return jax.ops.segment_sum(src, seg, n)
kernel_name = 'mk_gnn_resnorm_d1_gnn_r64_577a03'

def setup_inputs(seed: int=0):
    np.random.seed(seed)
    _w = jnp.asarray

    def _rec_inputs():
        import jax
        import jax.numpy as jnp
        _gk = jax.random.key(seed)
        x = -0.000202 + 1 * jax.random.normal(jax.random.fold_in(_gk, 1), (100000, 128), jnp.float32)
        src = jax.random.randint(jax.random.fold_in(_gk, 2), (50000,), 0, 100000, jnp.int32)
        dst = jax.random.randint(jax.random.fold_in(_gk, 3), (50000,), 0, 100000, jnp.int32)
        _o = jnp.argsort(dst, stable=True)
        src = src[_o]
        dst = dst[_o]
        edge_attr_64 = -8.16379e-05 + 0.999858 * jax.random.normal(jax.random.fold_in(_gk, 12), (50000, 64), jnp.float32)
        return (x, src, dst, edge_attr_64)
    x, src, dst, edge_attr_64 = _rec_inputs()

    def _L0_gnn_setup():
        import jax, jax.numpy as jnp
        import numpy as np
        N_NODES = 50000
        N_EDGES = 25000
        IN_NODE = 128
        IN_EDGE = 64
        OUT_F = 32
        HEADS = 4
        NEG_SLOPE = 0.2
        key = jax.random.key(seed)
        k = jax.random.split(key, 7)
        node_feats = jax.random.normal(k[0], (N_NODES, IN_NODE), dtype=jnp.float32)
        edge_feats = jax.random.normal(k[1], (N_EDGES, IN_EDGE), dtype=jnp.float32)
        src = jax.random.randint(k[2], (N_EDGES,), 0, N_NODES, dtype=jnp.int32)
        dst = jax.random.randint(k[3], (N_EDGES,), 0, N_NODES, dtype=jnp.int32)
        W_node = jax.random.normal(k[4], (IN_NODE, OUT_F * HEADS), dtype=jnp.float32) * 0.05
        W_edge = jax.random.normal(k[5], (IN_EDGE, OUT_F * HEADS), dtype=jnp.float32) * 0.05
        attn = jax.random.normal(k[6], (1, HEADS, 3 * OUT_F), dtype=jnp.float32) * 0.05
        return {'node_feats': node_feats, 'edge_feats': edge_feats, 'src': src, 'dst': dst, 'W_node': W_node, 'W_edge': W_edge, 'attn': attn}
    _L0_gnn_all = _L0_gnn_setup()
    _L0_gnn_in = {k: v for k, v in _L0_gnn_all.items() if k in ('W_node', 'W_edge', 'attn')}
    del _L0_gnn_all
    return {'x': x, 'src': src, 'dst': dst, 'edge_attr_64': edge_attr_64, 'L0_gnn_W_node': _L0_gnn_in['W_node'], 'L0_gnn_W_edge': _L0_gnn_in['W_edge'], 'L0_gnn_attn': _L0_gnn_in['attn']}

def reference(x, src, dst, edge_attr_64, L0_gnn_W_node, L0_gnn_W_edge, L0_gnn_attn):
    import jax
    import jax.numpy as jnp

    def _L0_gnn_ref(node_feats, edge_feats, src, dst, W_node, W_edge, attn):
        import jax, jax.numpy as jnp
        import numpy as np
        N_NODES = 50000
        N_EDGES = 25000
        IN_NODE = 128
        IN_EDGE = 64
        OUT_F = 32
        HEADS = 4
        NEG_SLOPE = 0.2
        N = node_feats.shape[0]
        H, F = (HEADS, OUT_F)
        h = (node_feats @ W_node).reshape(N, H, F)
        e = (edge_feats @ W_edge).reshape(-1, H, F)
        a = attn.reshape(H, 3 * F)
        a_src, a_dst, a_e = (a[:, :F], a[:, F:2 * F], a[:, 2 * F:])
        s_src = jnp.einsum('nhf,hf->nh', h, a_src)
        s_dst = jnp.einsum('nhf,hf->nh', h, a_dst)
        score = s_src[src] + s_dst[dst] + jnp.einsum('ehf,hf->eh', e, a_e)
        score = jnp.where(score >= 0, score, NEG_SLOPE * score)
        smax = jax.ops.segment_max(score, dst, num_segments=N)
        ex = jnp.exp(score - smax[dst])
        denom = jax.ops.segment_sum(ex, dst, num_segments=N)
        alpha = ex / denom[dst]
        msg = alpha[..., None] * h[src]
        agg = jax.ops.segment_sum(msg, dst, num_segments=N)
        deg = jax.ops.segment_sum(jnp.ones((dst.shape[0],), jnp.float32), dst, num_segments=N)
        out = agg / jnp.maximum(deg, 1.0)[:, None, None]
        return out.reshape(N, H * F)
    x = _layernorm(x + _L0_gnn_ref(x, edge_attr_64, src, dst, L0_gnn_W_node, L0_gnn_W_edge, L0_gnn_attn), axis=-1)
    return x

_drawn_inputs = setup_inputs


def setup_inputs(seed=0):
    import zlib

    import numpy as np

    out = dict(_drawn_inputs(seed))
    spreads = {}
    factors = {'edge_attr_64': 8.0, 'L0_gnn_W_edge': 8.0, 'L0_gnn_attn': 8.0}
    for name, (base, spread) in spreads.items():
        noise = np.random.default_rng([zlib.crc32(name.encode()), seed]).standard_normal(out[name].shape)
        drawn = base * np.exp(spread * noise) if base else spread * noise
        out[name] = jnp.asarray(drawn.astype(out[name].dtype))
    for name, factor in factors.items():
        out[name] = (out[name] * factor).astype(out[name].dtype)
    return out
```

```python
from contextlib import ExitStack

import concourse.bass as bass
from concourse import mybir

ALU = mybir.AluOpType
ACT = mybir.ActivationFunctionType
AX = mybir.AxisListType
F32 = mybir.dt.float32
I32 = mybir.dt.int32

P = 128
BIG = 1.0e30
NEG_SLOPE = 0.2
EPS = 1.0e-5


def gnn_residual_layernorm(nc, x, src, dst, edge_attr, w_node, w_edge, attn, out):
    N, D = x.shape
    E, DE = edge_attr.shape
    H = attn.shape[1]
    F = D // H
    ET = -(-E // P)
    GT = 23
    NG = ET // GT
    LAST = E - (ET - 1) * P
    HR = H + 1
    RR = HR * GT
    SKIP = 2 * N
    NB = -(-ET // P)
    ETP = NB * P
    assert NG * GT == ET and RR <= P and D == P and NG % 2 == 1

    XR = 45
    NR = XR * NG
    MAIN = P * NR
    TP = 104
    TR = (N - MAIN) // TP
    assert MAIN + TP * TR == N

    with ExitStack() as ctx:
        def sb(name, shape, dt=F32):
            return ctx.enter_context(nc.sbuf_tensor(name, shape, dt))

        def psum(name):
            return ctx.enter_context(nc.psum_tensor(name, [P, 512], F32))

        def sem(name):
            return ctx.enter_context(nc.semaphore(name))

        turned = [psum(f"turned{b}") for b in range(2)]
        hs_ps = [psum(f"hs_ps{b}") for b in range(2)]
        sums = [psum(f"sums{b}") for b in range(2)]
        dst_ps = psum("dst_ps")
        stage = psum("stage")

        ident = sb("ident", [P, P])
        w_all = sb("w_all", [P, D + H])
        w_dst = sb("w_dst", [P, H])
        w_edg = sb("w_edg", [P, H])
        w_e = sb("w_e", [DE, D])
        att = sb("att", [P, H, 3 * F])
        wtmp = sb("wtmp", [P, D])
        eps_t = sb("eps_t", [P, 1])
        m_last = sb("m_last", [P, 1])
        zero_t = sb("zero_t", [P, P])

        xs = [sb(f"xs{b}", [P, GT, D]) for b in range(2)]
        xd = [sb(f"xd{b}", [P, GT, D]) for b in range(2)]
        ef = [sb(f"ef{b}", [P, GT, DE]) for b in range(2)]
        hb = [sb(f"hb{b}", [P, GT, D + H]) for b in range(2)]
        zb = [sb(f"zb{b}", [P, GT, D]) for b in range(2)]
        xn = [sb(f"xn{b}", [P, XR, D]) for b in range(2)]
        xT = [sb(f"xT{b}", [P, 2 * P]) for b in range(2)]
        eT = [sb(f"eT{b}", [P, P]) for b in range(2)]
        same = [sb(f"same{b}", [P, 2, P]) for b in range(2)]
        prev = [sb(f"prev{b}", [P, D]) for b in range(2)]

        src_rows = sb("src_rows", [P, NB, P], I32)
        dst_rows = sb("dst_rows", [P, NB, P + 1], I32)
        dst_hr = sb("dst_hr", [P, NG, P + 1], I32)
        rows_f = sb("rows_f", [P, 3, NB, P])
        src_col = sb("src_col", [P, ETP], I32)
        dst_col = sb("dst_col", [P, ETP], I32)
        put_col = sb("put_col", [P, ETP], I32)
        dst2 = sb("dst2", [P, ETP, 2])
        now = [sb(f"now{b}", [P, 2, GT], I32) for b in range(2)]
        dst_now = sb("dst_now", [P, GT, 2])
        put_now = [sb(f"put_now{b}", [P, GT], I32) for b in range(2)]

        sc = sb("sc", [P, RR])
        s_low = sb("s_low", [RR, P])
        s_lr = sb("s_lr", [RR, P])
        s_same = sb("s_same", [RR, P])
        s_neg = sb("s_neg", [RR, P + 1])
        s_first = sb("s_first", [RR, P])
        s_fneg = sb("s_fneg", [RR, P])
        s_fmax = sb("s_fmax", [RR, P])
        s_tmax = sb("s_tmax", [RR, P])
        s_max = sb("s_max", [RR, P])
        s_arg = sb("s_arg", [RR, P])
        s_exp = sb("s_exp", [RR, P])
        s_den = sb("s_den", [RR, P])
        s_dtot = sb("s_dtot", [RR, P])
        c_max = sb("c_max", [RR, 1])
        c_fac = sb("c_fac", [RR, 1])
        c_wfac = sb("c_wfac", [RR, 1])
        c_den = sb("c_den", [RR, 1])
        r_mask = sb("r_mask", [1, HR, GT + 1])
        r_loc = sb("r_loc", [1, HR, GT + 1])
        r_max = sb("r_max", [1, HR, GT + 1])
        r_in = sb("r_in", [1, HR, GT])
        r_in2 = sb("r_in2", [1, HR, GT])
        r_wfac = sb("r_wfac", [1, HR, GT + 1])
        r_dloc = sb("r_dloc", [1, HR, GT + 1])
        r_den = sb("r_den", [1, HR, GT + 1])
        r_din = sb("r_din", [1, HR, GT])
        wgt = sb("wgt", [P, HR, GT])
        fac = sb("fac", [P, HR, GT])
        den = sb("den", [P, HR, GT])
        rec = sb("rec", [P, HR, GT])
        nrm = sb("nrm", [P, H, GT])

        st = sb("st", [P, XR, 6])
        st_sum = sb("st_sum", [P, XR])
        st_dif = sb("st_dif", [P, XR])
        st_m2 = sb("st_m2", [P, XR])
        st_d2 = sb("st_d2", [P, XR])
        st_var = sb("st_var", [P, XR])
        st_std = sb("st_std", [P, XR])
        rstd = sb("rstd", [P, XR])
        nbias = sb("nbias", [P, XR])

        z_dram = nc.dram_tensor("z_dram", (ET * P, D), F32, kind="Internal").ap()

        ld_w = sem("ld_w")
        ld_rows = sem("ld_rows")
        pool_c = sem("pool_c")
        pool_id = sem("pool_id")
        clear_rows = sem("clear_rows")
        pool_gate = sem("pool_gate")
        pe_gate = sem("pe_gate")
        dve_c = sem("dve_c")
        idx_pe = sem("idx_pe")
        idx_dve = sem("idx_dve")
        w_ready = sem("w_ready")
        now_ready = sem("now_ready")
        dst_ready = sem("dst_ready")
        got = [[sem(f"got{b}_{t}") for t in range(GT)] for b in range(2)]
        ef_in = [sem(f"ef_in{b}") for b in range(2)]
        ef_whole = sem("ef_whole")
        turned_full = sem("turned_full")
        xT_full = sem("xT_full")
        hs_full = sem("hs_full")
        h_full = sem("h_full")
        dst_full = sem("dst_full")
        same_full = sem("same_full")
        prev_full = sem("prev_full")
        sum_full = sem("sum_full")
        z_mul = sem("z_mul")
        z_full = sem("z_full")
        z_out = [sem(f"z_out{b}") for b in range(2)]
        stage_pe = sem("stage_pe")
        stage_dve = sem("stage_dve")
        arg_full = sem("arg_full")
        exp_full = sem("exp_full")
        x_in = [sem(f"x_in{b}") for b in range(2)]
        x_out = [sem(f"x_out{b}") for b in range(2)]
        rest_in = sem("rest_in")
        rest_out = sem("rest_out")
        var_full = sem("var_full")
        std_full = sem("std_full")
        rstd_full = sem("rstd_full")
        x_norm = sem("x_norm")
        z_in = [sem(f"z_in{b}") for b in range(2)]
        z_norm = sem("z_norm")
        put_ready = sem("put_ready")
        put_done = [sem(f"put_done{b}") for b in range(2)]

        x_nodes = x[0:MAIN, :].rearrange("(p r) f -> p r f", r=NR)
        out_nodes = out[0:MAIN, :].rearrange("(p r) f -> p r f", r=NR)
        x_rest = x[MAIN:N, :].rearrange("(p r) f -> p r f", r=TR)
        out_rest = out[MAIN:N, :].rearrange("(p r) f -> p r f", r=TR)
        ef_dram = edge_attr[0:(ET - 1) * P, :].rearrange("(k p) c -> p k c", p=P)
        z_tiles = z_dram.rearrange("(k p) f -> p k f", p=P)

        def window(t, offset, ap):
            return bass.AP(tensor=t.tensor, offset=offset, ap=ap)

        full = (NB - 1) * P
        odd = ET - 1 - full
        index_loads = [
            (src_rows[:, 0:NB - 1, :], window(src, 0, [[P, P], [P * P, NB - 1], [1, P]])),
            (src_rows[0:odd, NB - 1, :], window(src, full * P, [[P, odd], [1, P]])),
            (src_rows[odd:odd + 1, NB - 1, 0:LAST], window(src, (ET - 1) * P, [[LAST, 1], [1, LAST]])),
            (dst_rows[:, 0:NB - 1, :], window(dst, 0, [[P, P], [P * P, NB - 1], [1, P + 1]])),
            (dst_rows[0:odd, NB - 1, :], window(dst, full * P, [[P, odd], [1, P + 1]])),
            (dst_rows[odd:odd + 1, NB - 1, 0:LAST], window(dst, (ET - 1) * P, [[LAST, 1], [1, LAST]])),
        ]
        for h in range(HR):
            a, b = h * GT, (h + 1) * GT
            g = GT * P
            index_loads += [
                (dst_hr[a:b, 1:NG - 1, :], window(dst, g - 1, [[P, GT], [g, NG - 2], [1, P + 1]])),
                (dst_hr[a:a + 1, 0, 1:P + 1], window(dst, 0, [[P, 1], [1, P]])),
                (dst_hr[a + 1:b, 0, :], window(dst, P - 1, [[P, GT - 1], [1, P + 1]])),
                (dst_hr[a:b - 1, NG - 1, :], window(dst, (NG - 1) * g - 1, [[P, GT - 1], [1, P + 1]])),
                (dst_hr[b - 1:b, NG - 1, 0:LAST + 1], window(dst, (ET - 1) * P - 1, [[LAST + 1, 1], [1, LAST + 1]])),
            ]

        def in_pairs(eng, first, last, body):
            pairs = (last - first) // 2
            with eng.Fori(0, pairs) as j:
                for u in range(2):
                    i = first + u
                    body(j * 2 + i, i % 2, j + i // 2)
            for i in range(first + 2 * pairs, last):
                body(i, i % 2, i // 2)

        block = ctx.enter_context(nc.Block())

        @block.sync
        def _(sp):
            sp.dma_start(xn[1][0:TP, 0:TR, :], x_rest).then_inc(rest_in, 16)
            sp.wait_ge(clear_rows, 3)
            for to, of in index_loads:
                sp.dma_start(to, of).then_inc(ld_rows, 16)
            sp.dma_start(w_all[:, 0:D], w_node).then_inc(ld_w, 16)
            sp.dma_start(w_e[:], w_edge).then_inc(ld_w, 16)
            sp.dma_start(att[:], window(attn, 0, [[0, P], [3 * F, H], [1, 3 * F]])).then_inc(ld_w, 16)

            def load_nodes(i, par, uses):
                sp.dma_start(xn[par][:], x_nodes[:, bass.ds(i * XR, XR), :]).then_inc(x_in[par], 16)

            def load_edges(i, par, uses):
                sp.dma_start(ef[par][:], ef_dram[:, bass.ds(i * GT, GT), :]).then_inc(ef_in[par], 16)

            load_edges(0, 0, 0)
            load_nodes(0, 0, 0)
            load_edges(1, 1, 0)
            sp.wait_ge(rest_out, 16)
            load_nodes(1, 1, 0)

            def store_z(i, par, uses):
                sp.wait_ge(z_full, (i + 1) * GT)
                sp.dma_start(z_tiles[:, bass.ds(i * GT, GT), :], zb[par][:]).then_inc(z_out[par], 16)

            def round_(i, par, uses):
                sp.wait_ge(hs_full, (i - 1) * GT)
                load_edges(i, par, uses)
                sp.wait_ge(x_out[par], uses * 16)
                load_nodes(i, par, uses)
                store_z(i - 2, par, uses - 1)

            in_pairs(sp, 2, NG - 1, round_)
            i, par, uses = NG - 1, (NG - 1) % 2, (NG - 1) // 2
            sp.wait_ge(hs_full, (i - 1) * GT)
            sp.dma_start(ef[par][:, 0:GT - 1, :], ef_dram[:, i * GT:ET - 1, :]).then_inc(ef_whole, 16)
            sp.wait_ge(ef_whole, 16)
            sp.dma_start(ef[par][0:LAST, GT - 1, :], edge_attr[(ET - 1) * P:E, :]).then_inc(ef_in[par], 16)
            sp.wait_ge(x_out[par], uses * 16)
            load_nodes(i, par, uses)
            for i in range(NG - 3, NG):
                store_z(i, i % 2, i // 2)

            sp.wait_ge(z_out[0], 16 * ((NG + 1) // 2))
            sp.wait_ge(z_out[1], 16 * (NG // 2))

            def load_z(i, par, uses):
                for a, b in ((0, GT // 2), (GT // 2, GT)):
                    sp.dma_start(xs[par][:, a:b, :], z_tiles[:, bass.ds(i * GT + a, b - a), :]).then_inc(z_in[par], 16)

            load_z(0, 0, 0)
            load_z(1, 1, 0)

            def reload(i, par, uses):
                sp.wait_ge(put_done[par], uses * (16 * GT))
                load_z(i, par, uses)

            in_pairs(sp, 2, NG, reload)

        @block.gpsimd
        def _(pool):
            pool.memset(src_rows[:], 0).then_inc(clear_rows, 1)
            pool.memset(dst_rows[:], -1).then_inc(clear_rows, 1)
            pool.memset(dst_hr[:], -1).then_inc(clear_rows, 1)
            pool.memset(ident[:], 0.0).then_inc(pool_c, 1)
            pool.memset(m_last[:], 0.0).then_inc(pool_c, 1)
            pool.wait_ge(pool_c, 2)
            nc.gpsimd.affine_select(out=ident[:], in_=ident[:], compare_op=ALU.not_equal, fill=1.0, base=0,
                                    pattern=[[-1, P]], channel_multiplier=1).then_inc(pool_id, 1)
            nc.gpsimd.affine_select(out=m_last[:], in_=m_last[:], compare_op=ALU.not_equal, fill=1.0,
                                    base=-(P - 1), pattern=[[0, 1]], channel_multiplier=1).then_inc(pool_id, 1)

            def gather(i, par, uses, again=True):
                pool.wait_ge(now_ready, i + 1)
                pool.sem_inc(pool_gate, 1)
                for t in range(GT):
                    if again:
                        pool.wait_ge(z_full, (i - 2) * GT + (t + 1))
                        pool.sem_inc(pool_gate, 1)
                    for k, rows in enumerate((xs, xd)):
                        nc.gpsimd.indirect_dma_start(
                            rows[par][:, t, :], None, x,
                            bass.IndirectOffsetOnAxis(ap=now[par][:, k, t:t + 1], axis=0)).then_inc(got[par][t], 16)

            gather(0, 0, 0, False)
            gather(1, 1, 0, False)
            in_pairs(pool, 2, NG, gather)

            pool.wait_ge(rest_out, 16)
            pool.wait_ge(x_out[0], 16 * ((NG + 1) // 2))
            pool.wait_ge(x_out[1], 16 * (NG // 2))

            def scatter(i, par, uses):
                pool.wait_ge(put_ready, i + 1)
                pool.sem_inc(pool_gate, 1)
                for t in range(GT):
                    pool.wait_ge(z_norm, i * GT + (t + 1))
                    pool.sem_inc(pool_gate, 1)
                    nc.gpsimd.indirect_dma_start(
                        out, bass.IndirectOffsetOnAxis(ap=put_now[par][:, t:t + 1], axis=0),
                        xs[par][:, t, :], None, bounds_check=N - 1, oob_is_err=False).then_inc(put_done[par], 16)

            in_pairs(pool, 0, NG, scatter)
            pool.wait_ge(put_done[0], 16 * GT * ((NG + 1) // 2))
            pool.wait_ge(put_done[1], 16 * GT * (NG // 2))

        @block.tensor
        def _(pe):
            pe.wait_ge(pool_id, 2)
            pe.wait_ge(idx_dve, 1)
            for k in range(3):
                if k:
                    pe.wait_ge(idx_dve, k + 1)
                for b in range(NB):
                    mm = pe.transpose(stage[:, b * P:(b + 1) * P], rows_f[:, k, b, :], ident[:])
                mm.then_inc(idx_pe, 1)
            pe.wait_ge(w_ready, 1)
            pe.matmul(sums[1][:, 0:D], zero_t[:], zero_t[:], start=True, stop=True)

            def turn_in(i, par, uses, t):
                k = i * GT + t
                b = (par * GT + t) % 2
                if t == 0:
                    pe.wait_ge(ef_in[par], uses * 16 + 16)
                pe.wait_ge(got[par][t], uses * 32 + 32)
                pe.wait_ge(xT_full, k * 2 - 2) if not isinstance(k, int) or k >= 2 else None
                pe.transpose(turned[b][:, 0:P], xs[par][:, t, :], ident[:])
                pe.transpose(turned[b][:, P:2 * P], xd[par][:, t, :], ident[:])
                pe.transpose(turned[b][0:DE, 2 * P:3 * P], ef[par][:, t, :], ident[:]).then_inc(turned_full, 1)

            def project(i, par, uses, t):
                k = i * GT + t
                b = (par * GT + t) % 2
                pe.wait_ge(xT_full, k * 2 + 2)
                if not isinstance(k, int) or k >= 2:
                    pe.wait_ge(h_full, k - 1)
                pe.matmul(hs_ps[b][:, 0:D + H], xT[b][:, 0:P], w_all[:], start=True, stop=False,
                          skip_group_check=True)
                pe.matmul(hs_ps[b][:, D:D + H], xT[b][:, P:2 * P], w_dst[:], start=False, stop=False,
                          skip_group_check=True)
                pe.matmul(hs_ps[b][:, D:D + H], eT[b][:], w_edg[:], start=False, stop=True,
                          skip_group_check=True).then_inc(hs_full, 1)

            def spread_dst(i, par, t):
                k = i * GT + t
                if not isinstance(k, int) or k >= 1:
                    pe.wait_ge(same_full, k)
                pe.transpose(dst_ps[:, 0:P], dst_now[:, t:t + 1, 0].to_broadcast([P, P]),
                             ident[:]).then_inc(dst_full, 1)

            def add_up(i, par, t):
                k = i * GT + t
                b = (par * GT + t) % 2
                pe.wait_ge(same_full, k + 1)
                pe.matmul(sums[b][:, 0:D], same[b][:, 0, :], hb[par][:, t, 0:D], start=True, stop=False)
                pe.wait_ge(prev_full, k + 1)
                pe.matmul(sums[b][:, 0:D], same[b][:, 1, :], prev[b][:], start=False, stop=True).then_inc(sum_full, 1)

            def softmax_turns(i):
                n = i * 6
                pe.wait_ge(stage_dve, n + 1)
                pe.transpose(stage[0:RR, 0:P], sc[:], ident[:]).then_inc(stage_pe, 1)
                pe.wait_ge(stage_dve, n + 2)
                for q, col in enumerate((s_tmax[:, P - 1:P], s_first[:, P - 1:P], s_same[:, 0:1])):
                    mm = pe.transpose(stage[0:1, P + q * RR:P + (q + 1) * RR], col, ident[0:RR, 0:RR])
                mm.then_inc(stage_pe, 1)
                pe.wait_ge(stage_dve, n + 3)
                pe.sem_inc(pe_gate, 1)
                pe.transpose(stage[0:RR, 0:1], r_in2[:].rearrange("o h t -> o (h t)"), ident[0:1, 0:1]).then_inc(stage_pe, 1)
                pe.wait_ge(stage_dve, n + 4)
                pe.transpose(stage[:, 0:RR], s_exp[:], ident[0:RR, 0:RR])
                pe.transpose(stage[:, RR:2 * RR], c_fac[:].to_broadcast([RR, P]), ident[0:RR, 0:RR])
                pe.transpose(stage[0:1, 2 * RR:3 * RR], s_den[:, P - 1:P], ident[0:RR, 0:RR])
                pe.transpose(stage[0:1, 3 * RR:4 * RR], c_wfac[:], ident[0:RR, 0:RR]).then_inc(stage_pe, 1)
                pe.wait_ge(stage_dve, n + 5)
                pe.sem_inc(pe_gate, 1)
                pe.transpose(stage[0:RR, 0:1], r_din[:].rearrange("o h t -> o (h t)"), ident[0:1, 0:1]).then_inc(stage_pe, 1)
                pe.wait_ge(stage_dve, n + 6)
                pe.transpose(stage[:, 0:RR], s_dtot[:], ident[0:RR, 0:RR]).then_inc(stage_pe, 1)

            def round_(i, par, uses, edges=True, before=True):
                if before:
                    pe.wait_ge(dst_ready, i)
                    spread_dst(i - 1, 1 - par, 0)
                for t in range(GT):
                    if edges:
                        turn_in(i, par, uses, t)
                    if before:
                        add_up(i - 1, 1 - par, t)
                        if t + 1 < GT:
                            spread_dst(i - 1, 1 - par, t + 1)
                    if edges:
                        project(i, par, uses, t)
                if edges:
                    softmax_turns(i)

            round_(0, 0, 0, before=False)
            in_pairs(pe, 1, NG, round_)
            round_(NG, NG % 2, NG // 2, edges=False)

        @block.scalar
        def _(act):
            def norm_rows(rows, n, first_sem):
                for r in range(n):
                    mm = act.activation(rows[r], rows[r], ACT.Identity, scale=rstd[0:rows[r].shape[0], r:r + 1],
                                        bias=nbias[0:rows[r].shape[0], r:r + 1])
                    if first_sem is not None:
                        mm.then_inc(first_sem, 1)
                return mm

            def std_of(n, cols, parts=P):
                act.wait_ge(var_full, n + 1)
                act.activation(st_std[0:parts, 0:cols], st_var[0:parts, 0:cols], ACT.Sqrt, scale=1.0 / D,
                               bias=eps_t[0:parts, :]).then_inc(std_full, 1)

            std_of(0, TR, TP)
            act.wait_ge(rstd_full, 1)
            norm_rows([xn[1][0:TP, r, :] for r in range(TR)], TR, None).then_inc(x_norm, 1)
            act.wait_ge(x_norm, 1)
            act.dma_start(out_rest, xn[1][0:TP, 0:TR, :]).then_inc(rest_out, 16)

            def round_(i, par, uses, edges=True, nodes=True):
                for t in range(GT):
                    b = (par * GT + t) % 2
                    k = i * GT + t
                    if edges:
                        act.wait_ge(turned_full, k + 1)
                        act.activation(xT[b][:], turned[b][:, 0:2 * P], ACT.Copy).then_inc(xT_full, 1)
                        act.activation(eT[b][0:DE, :], turned[b][0:DE, 2 * P:3 * P], ACT.Copy).then_inc(xT_full, 1)
                    if nodes and t < XR // 3:
                        if t == 0:
                            act.wait_ge(rstd_full, i + 1)
                        for r in range(3 * t, 3 * t + 3):
                            row = xn[1 - par][:, r, :]
                            last = act.activation(row, row, ACT.Identity, scale=rstd[:, r:r + 1],
                                                  bias=nbias[:, r:r + 1])
                        if t == XR // 3 - 1:
                            last.then_inc(x_norm, 1)
                    if nodes and t == XR // 3:
                        act.wait_ge(x_norm, i + 1)
                        act.dma_start(out_nodes[:, bass.ds((i - 1) * XR, XR), :], xn[1 - par][:]).then_inc(x_out[1 - par], 16)
                    if edges:
                        act.wait_ge(hs_full, k + 1)
                        act.activation(hb[par][:, t, :], hs_ps[b][:, 0:D + H], ACT.Copy).then_inc(h_full, 1)
                if edges:
                    std_of(i + 1, XR)
                    act.wait_ge(arg_full, i + 1)
                    act.activation(s_exp[:], s_arg[:], ACT.Exp).then_inc(exp_full, 1)
                    act.activation(c_fac[:], s_max[:, 0:1], ACT.Exp, scale=-1.0, bias=c_max[:]).then_inc(exp_full, 1)

            round_(0, 0, 0, nodes=False)
            in_pairs(act, 1, NG, round_)
            round_(NG, NG % 2, NG // 2, edges=False)

            def norm_z(i, par, uses):
                std_of(i + (NG + 1), GT)
                act.wait_ge(rstd_full, i + (NG + 2))
                for t in range(GT):
                    act.activation(xs[par][:, t, :], xs[par][:, t, :], ACT.Identity, scale=rstd[:, t:t + 1],
                                   bias=nbias[:, t:t + 1]).then_inc(z_norm, 1)

            in_pairs(act, 0, NG, norm_z)

        @block.vector
        def _(dve):
            class Chain:
                base, n = 0, 0

            def link(ins):
                Chain.n += 1
                ins.then_inc(dve_c, 1)
                dve.wait_ge(dve_c, Chain.base + Chain.n)

            def fork(ins):
                Chain.n += 1
                ins.then_inc(dve_c, 1)

            def statistics(cols, parts=P):
                s = [st[0:parts, 0:cols, q] for q in range(6)]
                a = [v[0:parts, 0:cols] for v in (st_sum, st_dif, st_m2, st_d2, st_var)]
                fork(dve.tensor_tensor(a[0], s[1], s[4], ALU.add))
                fork(dve.tensor_tensor(a[1], s[1], s[4], ALU.subtract))
                link(dve.tensor_tensor(a[2], s[2], s[5], ALU.add))
                link(dve.scalar_tensor_tensor(a[3], a[1], D / 4.0, a[1], ALU.mult, ALU.mult))
                dve.tensor_tensor(a[4], a[2], a[3], ALU.add).then_inc(var_full, 1)

            def scales(n, cols, parts=P):
                dve.wait_ge(std_full, n + 1)
                link(dve.reciprocal(rstd[0:parts, 0:cols], st_std[0:parts, 0:cols]))
                dve.scalar_tensor_tensor(nbias[0:parts, 0:cols], st_sum[0:parts, 0:cols], -0.5,
                                         rstd[0:parts, 0:cols], ALU.mult, ALU.mult).then_inc(rstd_full, 1)

            fork(dve.memset(eps_t[:], EPS))
            fork(dve.memset(zero_t[:], 0.0))
            fork(dve.memset(sc[:], 0.0))
            fork(dve.memset(s_neg[:], -BIG))
            fork(dve.memset(r_mask[:], -BIG))
            fork(dve.memset(r_max[:], -BIG))
            fork(dve.memset(r_den[:], 0.0))
            fork(dve.memset(r_wfac[:], 0.0))
            fork(dve.memset(eT[0][:], 0.0))
            fork(dve.memset(eT[1][:], 0.0))
            link(dve.memset(w_edg[:], 0.0))

            dve.wait_ge(ld_rows, 16 * len(index_loads))
            fork(dve.tensor_copy(rows_f[:, 0], src_rows[:]))
            fork(dve.tensor_copy(rows_f[:, 1], dst_rows[:, :, 0:P]))
            link(dve.tensor_tensor(rows_f[:, 2], dst_rows[:, :, 0:P], dst_rows[:, :, 1:P + 1], ALU.is_equal))
            dve.scalar_tensor_tensor(rows_f[:, 2], rows_f[:, 2], float(SKIP), rows_f[:, 1],
                                     ALU.mult, ALU.add).then_inc(idx_dve, 1)
            dve.wait_ge(idx_pe, 1)
            dve.tensor_copy(src_col[:], stage[:]).then_inc(idx_dve, 1)
            dve.wait_ge(idx_pe, 2)
            fork(dve.tensor_copy(dst2[:, :, 0], stage[:]))
            fork(dve.memset(dst2[:, 0:1, 1], -5.0))
            fork(dve.tensor_scalar(dst2[:, 1:ETP, 1], stage[:, 0:ETP - 1], 5.0, m_last[:], ALU.add, ALU.mult))
            dve.tensor_scalar(dst_col[:], stage[:], 0.0, None, ALU.max).then_inc(idx_dve, 1)
            dve.wait_ge(idx_pe, 3)
            fork(dve.tensor_copy(put_col[:], stage[:]))
            dve.wait_ge(dve_c, Chain.n)
            link(dve.tensor_scalar(dst2[:, 1:ETP, 1], dst2[:, 1:ETP, 1], -5.0, None, ALU.add))

            def group_indices(i, par):
                dve.wait_ge(idx_dve, 3) if isinstance(i, int) and i < 2 else None
                dve.tensor_copy(now[par][:, 0, :], src_col[:, bass.ds(i * GT, GT)])
                dve.tensor_copy(now[par][:, 1, :], dst_col[:, bass.ds(i * GT, GT)]).then_inc(now_ready, 1)

            group_indices(0, 0)
            group_indices(1, 1)

            dve.wait_ge(ld_w, 48)
            for to, w, part, rows in ((w_all[:, D:D + H], w_all[:, 0:D], 0, P), (w_dst[:], w_all[:, 0:D], 1, P),
                                      (w_edg[0:DE, :], w_e[:], 2, DE)):
                link(dve.tensor_tensor(wtmp[0:rows, :].rearrange("k (h f) -> k h f", h=H),
                                       w.rearrange("k (h f) -> k h f", h=H),
                                       att[0:rows, :, part * F:(part + 1) * F], ALU.mult))
                link(dve.tensor_reduce(to, wtmp[0:rows, :].rearrange("k (h f) -> k h f", h=H), AX.X, ALU.add))
            dve.memset(prev[0][:], 0.0).then_inc(w_ready, 1)

            dve.wait_ge(rest_in, 16)
            for r in range(TR):
                ins = dve.bn_stats(st[0:TP, r, :], xn[1][0:TP, r, :])
            link(ins)
            statistics(TR, TP)
            scales(0, TR, TP)

            def softmax(i, par):
                n = i * 6
                D_ = dst_hr[0:RR, bass.ds(i, 1), :].rearrange("r o e -> r (o e)")
                here, before = D_[:, 1:P + 1], D_[:, 0:P]
                dve.wait_ge(h_full, (i + 1) * GT)
                dve.tensor_copy(sc[:, 0:H * GT].rearrange("p (h t) -> p h t", h=H),
                                hb[par][:, :, D:D + H].rearrange("p t h -> p h t")).then_inc(stage_dve, 1)
                fork(dve.tensor_tensor(s_same[:], here, before, ALU.is_equal))
                link(dve.tensor_tensor(s_first[:], here, D_[:, 0:1].to_broadcast([RR, P]), ALU.is_equal))
                fork(dve.tensor_scalar(s_neg[:, 0:P], s_same[:], -1.0, BIG, ALU.add, ALU.mult))
                fork(dve.tensor_scalar(s_fneg[:], s_first[:], -1.0, BIG, ALU.add, ALU.mult))
                dve.wait_ge(stage_pe, n + 1)
                link(dve.tensor_scalar(s_low[:], stage[0:RR, 0:P], NEG_SLOPE, None, ALU.mult))
                link(dve.tensor_tensor(s_lr[:], s_low[:], stage[0:RR, 0:P], ALU.max))
                link(dve.tensor_tensor_scan(s_fmax[:], s_neg[:, 0:P], s_lr[:], -BIG, ALU.add, ALU.max))
                dve.tensor_tensor_scan(s_tmax[:, ::-1], s_neg[:, 1:P + 1][:, ::-1], s_fmax[:, ::-1], -BIG,
                                       ALU.add, ALU.max).then_inc(stage_dve, 1)
                fork(dve.tensor_copy(r_loc[:, :, 0:1], r_max[:, :, GT:GT + 1]))
                dve.wait_ge(stage_pe, n + 2)
                row = [stage[0:1, P + q * RR:P + (q + 1) * RR].rearrange("o (h t) -> o h t", h=HR) for q in range(3)]
                fork(dve.tensor_copy(r_loc[:, :, 1:GT + 1], row[0]))
                fork(dve.tensor_scalar(r_mask[:, :, 1:GT + 1], row[1], -1.0, BIG, ALU.add, ALU.mult))
                link(dve.tensor_scalar(r_in[:], row[2], -1.0, BIG, ALU.add, ALU.mult))
                link(dve.tensor_tensor_scan(r_max[:].rearrange("o h t -> o (h t)"),
                                            r_mask[:].rearrange("o h t -> o (h t)"),
                                            r_loc[:].rearrange("o h t -> o (h t)"), -BIG, ALU.add, ALU.max))
                dve.tensor_tensor(r_in2[:], r_in[:], r_max[:, :, 0:GT], ALU.add).then_inc(stage_dve, 1)
                dve.wait_ge(stage_pe, n + 3)
                link(dve.tensor_copy(c_max[:], stage[0:RR, 0:1]))
                link(dve.scalar_tensor_tensor(s_max[:], s_fneg[:], c_max[:], s_tmax[:], ALU.add, ALU.max))
                dve.tensor_tensor(s_arg[:], s_lr[:], s_max[:], ALU.subtract).then_inc(arg_full, 1)
                scales(i + 1, XR)
                dve.wait_ge(exp_full, i * 2 + 2)
                fork(dve.tensor_tensor(c_wfac[:], s_first[:, P - 1:P], c_fac[:], ALU.mult))
                dve.tensor_tensor_scan(s_den[:], s_same[:], s_exp[:], 0.0, ALU.mult, ALU.add).then_inc(stage_dve, 1)
                fork(dve.tensor_copy(r_dloc[:, :, 0:1], r_den[:, :, GT:GT + 1]))
                dve.wait_ge(stage_pe, n + 4)
                fork(dve.tensor_copy(r_dloc[:, :, 1:GT + 1],
                                     stage[0:1, 2 * RR:3 * RR].rearrange("o (h t) -> o h t", h=HR)))
                link(dve.tensor_copy(r_wfac[:, :, 1:GT + 1],
                                     stage[0:1, 3 * RR:4 * RR].rearrange("o (h t) -> o h t", h=HR)))
                link(dve.tensor_tensor_scan(r_den[:].rearrange("o h t -> o (h t)"),
                                            r_wfac[:].rearrange("o h t -> o (h t)"),
                                            r_dloc[:].rearrange("o h t -> o (h t)"), 0.0, ALU.mult, ALU.add))
                fork(dve.tensor_copy(wgt[:].rearrange("p h t -> p (h t)"), stage[:, 0:RR]))
                fork(dve.tensor_copy(fac[:].rearrange("p h t -> p (h t)"), stage[:, RR:2 * RR]))
                dve.tensor_copy(r_din[:], r_den[:, :, 0:GT]).then_inc(stage_dve, 1)
                dve.wait_ge(stage_pe, n + 5)
                link(dve.tensor_tensor(c_den[:], stage[0:RR, 0:1], c_fac[:], ALU.mult))
                dve.scalar_tensor_tensor(s_dtot[:], s_first[:], c_den[:], s_den[:], ALU.mult,
                                         ALU.add).then_inc(stage_dve, 1)
                msg = hb[par][:, :, 0:D].rearrange("p t (h f) -> p t h f", h=H)
                dve.tensor_copy(dst_now[:], dst2[:, bass.ds(i * GT, GT), :]).then_inc(dst_ready, 1)
                fork(dve.tensor_tensor(msg, msg, wgt[:, 0:H, :].rearrange("p h t -> p t h").unsqueeze(3)
                                       .to_broadcast([P, GT, H, F]), ALU.mult))
                dve.wait_ge(stage_pe, n + 6)
                link(dve.tensor_scalar(den[:].rearrange("p h t -> p (h t)"), stage[:, 0:RR], 0.5, None, ALU.max))
                link(dve.reciprocal(rec[:], den[:]))
                link(dve.tensor_tensor(nrm[:], rec[:, 0:H, :], rec[:, H:HR, :].to_broadcast([P, H, GT]), ALU.mult))

            def match(i, par, t):
                k = i * GT + t
                b = (par * GT + t) % 2
                dve.wait_ge(dst_full, k + 1)
                dve.tensor_tensor(same[b][:], dst_ps[:, 0:P].unsqueeze(1).to_broadcast([P, 2, P]),
                                  dst_now[:, t, :].unsqueeze(2)
                                  .to_broadcast([P, 2, P]), ALU.is_equal).then_inc(same_full, 1)

            def carry(i, par, t):
                k = i * GT + t
                b = (par * GT + t) % 2
                if not isinstance(k, int) or k >= 1:
                    dve.wait_ge(sum_full, k)
                dve.tensor_tensor(prev[b][:].rearrange("p (h f) -> p h f", h=H),
                                  sums[1 - b][:, 0:D].rearrange("p (h f) -> p h f", h=H),
                                  fac[:, 0:H, t:t + 1].to_broadcast([P, H, F]), ALU.mult).then_inc(prev_full, 1)

            def z_times(i, par, uses, t):
                k = i * GT + t
                b = (par * GT + t) % 2
                dve.wait_ge(sum_full, k + 1)
                if t == 0 and not (isinstance(i, int) and i < 2):
                    dve.wait_ge(z_out[par], uses * 16)
                dve.tensor_tensor(zb[par][:, t, :].rearrange("p (h f) -> p h f", h=H),
                                  sums[b][:, 0:D].rearrange("p (h f) -> p h f", h=H),
                                  nrm[:, :, t:t + 1].to_broadcast([P, H, F]), ALU.mult).then_inc(z_mul, 1)

            def z_plus(i, par, t):
                k = i * GT + t
                dve.wait_ge(z_mul, k + 1)
                dve.tensor_tensor(zb[par][:, t, :], zb[par][:, t, :], xd[par][:, t, :], ALU.add).then_inc(z_full, 1)

            def round_(i, par, uses, edges=True, before=True):
                q, qu = 1 - par, (uses if par else uses - 1)
                skip = GT - XR // 3
                for t in range(GT):
                    if before:
                        match(i - 1, q, t)
                        carry(i - 1, q, t)
                        if t:
                            z_times(i - 1, q, qu, t - 1)
                    if edges and t >= skip:
                        if t == skip:
                            dve.wait_ge(x_in[par], uses * 16 + 16)
                        for r in range(3 * (t - skip), 3 * (t - skip) + 3):
                            ins = dve.bn_stats(st[:, r, :], xn[par][:, r, :])
                        if t == GT - 1:
                            fork(ins)
                    if before and t:
                        z_plus(i - 1, q, t - 1)
                if before:
                    z_times(i - 1, q, qu, GT - 1)
                    z_plus(i - 1, q, GT - 1)
                if edges:
                    dve.wait_ge(dve_c, Chain.base + Chain.n)
                    statistics(XR)
                    softmax(i, par)
                    if not isinstance(i, int) or i + 2 < NG:
                        group_indices(i + 2, par)

            Chain.base, Chain.n = Chain.base + Chain.n, 0
            round_(0, 0, 0, before=False)
            per = Chain.n
            start = Chain.base + per

            def counted_round(i, par, uses):
                Chain.base, Chain.n = (i - 1) * per + start, 0
                round_(i, par, uses)
                assert Chain.n == per

            in_pairs(dve, 1, NG - 2, counted_round)
            counted_round(NG - 2, (NG - 2) % 2, (NG - 2) // 2)
            counted_round(NG - 1, (NG - 1) % 2, (NG - 1) // 2)
            Chain.base, Chain.n = (NG - 1) * per + start, 0
            round_(NG, NG % 2, NG // 2, edges=False)

            start_z = Chain.base + Chain.n

            def stats_z(i, par, uses):
                if not isinstance(i, int) or i >= 2:
                    dve.wait_ge(put_done[par], uses * (16 * GT))
                dve.tensor_copy(put_now[par][:], put_col[:, bass.ds(i * GT, GT)]).then_inc(put_ready, 1)
                dve.wait_ge(z_in[par], uses * 32 + 32)
                for t in range(GT):
                    ins = dve.bn_stats(st[:, t, :], xs[par][:, t, :])
                link(ins)
                if isinstance(i, int) and i == 0:
                    pass
                else:
                    dve.wait_ge(z_norm, i * GT)
                statistics(GT)
                scales(i + (NG + 1), GT)

            def counted_z(i, par, uses):
                Chain.base, Chain.n = i * per_z + start_z, 0
                stats_z(i, par, uses)
                assert Chain.n == per_z

            per_z = 6
            counted_z(0, 0, 0)
            counted_z(1, 1, 0)
            in_pairs(dve, 2, NG, counted_z)


_INS = ['x', 'src', 'dst', 'edge_attr_64', 'L0_gnn_W_node', 'L0_gnn_W_edge', 'L0_gnn_attn']


def kernel(**inputs):
    import numpy as _np
    import concourse.bacc as _bacc
    from concourse import mybir as _mybir
    from concourse.bass_utils import run_bass_kernel_spmd as _run

    nc = _bacc.Bacc("TRN2", target_bir_lowering=False, num_devices=1)
    arrays, args = {}, []
    for name in _INS:
        a = _np.ascontiguousarray(inputs[name])
        arrays[f"in_{name}_dram"] = a
        args.append(nc.dram_tensor(f"in_{name}_dram", a.shape, _mybir.dt.from_np(a.dtype), kind="ExternalInput").ap())
    out = nc.dram_tensor("out_0_dram", inputs['x'].shape, _mybir.dt.float32, kind="ExternalOutput").ap()
    gnn_residual_layernorm(nc, *args, out)
    r = _run(nc, [arrays], core_ids=[0])
    return r.results[0]["out_0_dram"]
```

```python
from contextlib import ExitStack

import concourse.bass as bass
from concourse import mybir

ALU = mybir.AluOpType
ACT = mybir.ActivationFunctionType
AX = mybir.AxisListType
F32 = mybir.dt.float32
I32 = mybir.dt.int32

P = 128
BIG = 1.0e30
NEG_SLOPE = 0.2
EPS = 1.0e-5


def gnn_residual_layernorm(nc, x, src, dst, edge_attr, w_node, w_edge, attn, out):
    N, D = x.shape
    E, DE = edge_attr.shape
    H = attn.shape[1]
    F = D // H
    ET = -(-E // P)
    GT = 23
    NG = ET // GT
    LAST = E - (ET - 1) * P
    HR = H + 1
    RR = HR * GT
    SKIP = 2 * N
    NB = -(-ET // P)
    ETP = NB * P
    assert NG * GT == ET and RR <= P and D == P and NG % 2 == 1

    NX = NG - 2
    XR = 51
    NR = XR * NX
    ZT = 2 * GT
    NZ = -(-ET // ZT)
    AS = (GT + 1) // 2
    FILL = 6
    HW = D + H
    MAIN = P * NR
    TP = 104
    TR = (N - MAIN) // TP
    assert MAIN + TP * TR == N and ZT <= XR and NX % 2 == 1 and NZ == NX // 2 + 2
    assert AS % 2 == 0 and 2 * DE == P

    with ExitStack() as ctx:
        def sb(name, shape, dt=F32):
            return ctx.enter_context(nc.sbuf_tensor(name, shape, dt))

        def psum(name):
            return ctx.enter_context(nc.psum_tensor(name, [P, 512], F32))

        def sem(name):
            return ctx.enter_context(nc.semaphore(name))

        turned = [psum(f"turned{b}") for b in range(2)]
        hs_ps = [psum(f"hs_ps{b}") for b in range(2)]
        sums = [psum(f"sums{b}") for b in range(2)]
        dst_ps = psum("dst_ps")
        stage = psum("stage")

        ident = sb("ident", [P, P])
        w_all = sb("w_all", [P, D + H])
        w_dst = sb("w_dst", [P, H])
        w_edg = sb("w_edg", [P, 2, H])
        w_ea = sb("w_ea", [P, H])
        w_e = sb("w_e", [P, D])
        att = sb("att", [P, H, 3 * F])
        wtmp = sb("wtmp", [P, D])
        eps_t = sb("eps_t", [P, 1])
        m_last = sb("m_last", [P, 1])
        zero_t = sb("zero_t", [P, P])

        xs = [sb(f"xs{b}", [P, GT, D]) for b in range(2)]
        xd = [sb(f"xd{b}", [P, GT, D]) for b in range(2)]
        ef = [sb(f"ef{b}", [P, GT, DE]) for b in range(2)]
        hb = [sb(f"hb{b}", [P, GT, D + H]) for b in range(2)]
        zb = [sb(f"zb{b}", [P, GT, D]) for b in range(2)]
        xn = [sb(f"xn{b}", [P, XR, D]) for b in range(2)]
        xT = [sb(f"xT{b}", [P, 4 * P]) for b in range(2)]
        eT = [sb(f"eT{b}", [P, P]) for b in range(2)]
        same = [sb(f"same{b}", [P, 2, P]) for b in range(2)]
        prev = [sb(f"prev{b}", [P, D]) for b in range(2)]

        rows_f = zb[0][:, 0:3 * NB, :].rearrange("p (k b) e -> p k b e", k=3)

        rows_i = zb[1][:].rearrange("p t f -> p (t f)").bitcast(I32)
        src_rows = rows_i[:, 0:NB * P].rearrange("p (b e) -> p b e", b=NB)
        dst_rows = rows_i[:, NB * P:NB * (2 * P + 1)].rearrange("p (b e) -> p b e", b=NB)
        dst_hr = sb("dst_hr", [P, NG, P + 1], I32)
        src_col = sb("src_col", [P, ETP], I32)
        dst_col = sb("dst_col", [P, ETP], I32)
        put_col = sb("put_col", [P, ETP], I32)
        dst2 = sb("dst2", [P, ETP, 2])
        now = [sb(f"now{b}", [P, 2, GT], I32) for b in range(2)]
        dst_now = [sb(f"dst_now{b}", [P, GT, 2]) for b in range(2)]
        put_now = [sb(f"put_now{b}", [P, ZT], I32) for b in range(2)]

        sc = sb("sc", [P, RR])
        s_lr = sb("s_lr", [RR, P])
        s_same = sb("s_same", [RR, P])
        s_neg = sb("s_neg", [RR, P + 1])
        s_first = sb("s_first", [RR, P])
        s_fneg = sb("s_fneg", [RR, P])
        s_fmax = sb("s_fmax", [RR, P])
        s_tmax = sb("s_tmax", [RR, P])
        s_max = sb("s_max", [RR, P])
        s_arg = sb("s_arg", [RR, P])
        s_exp = sb("s_exp", [RR, P])
        s_den = sb("s_den", [RR, P])
        s_dtot = sb("s_dtot", [RR, P])
        c_max = sb("c_max", [RR, 1])
        c_fac = sb("c_fac", [RR, 1])
        c_wfac = sb("c_wfac", [RR, 1])
        c_den = sb("c_den", [RR, 1])
        r_mask = sb("r_mask", [1, HR, GT + 1])
        r_loc = sb("r_loc", [1, HR, GT + 1])
        r_max = sb("r_max", [1, HR, GT + 1])
        r_in = sb("r_in", [1, HR, GT])
        r_in2 = sb("r_in2", [1, HR, GT])
        r_wfac = sb("r_wfac", [1, HR, GT + 1])
        r_dloc = sb("r_dloc", [1, HR, GT + 1])
        r_den = sb("r_den", [1, HR, GT + 1])
        r_din = sb("r_din", [1, HR, GT])
        wgt = sb("wgt", [P, HR, GT])
        fac = [sb(f"fac{b}", [P, HR, GT]) for b in range(2)]
        den = sb("den", [P, HR, GT])
        rec = sb("rec", [P, H, GT])
        nrm = [sb(f"nrm{b}", [P, H, GT]) for b in range(2)]

        st = sb("st", [P, XR, 6])
        st_sum = sb("st_sum", [P, XR])
        st_dif = sb("st_dif", [P, XR])
        st_m2 = sb("st_m2", [P, XR])
        st_d2 = sb("st_d2", [P, XR])
        st_var = sb("st_var", [P, XR])
        st_std = sb("st_std", [P, XR])
        rstd = sb("rstd", [P, XR])
        nbias = sb("nbias", [P, XR])

        z_dram = nc.dram_tensor("z_dram", (ET * P, D), F32, kind="Internal").ap()

        ld_w = sem("ld_w")
        ld_first = sem("ld_first")
        ld_rows = sem("ld_rows")
        ld_hr = sem("ld_hr")
        pool_c = sem("pool_c")
        pool_id = sem("pool_id")
        clear_rows = sem("clear_rows")
        pool_gate = sem("pool_gate")
        pe_gate = sem("pe_gate")
        dve_c = sem("dve_c")
        idx_pe = sem("idx_pe")
        idx_dve = sem("idx_dve")
        w_ready = sem("w_ready")
        now_ready = sem("now_ready")
        dst_ready = sem("dst_ready")
        got = [[sem(f"got{b}_{t}") for t in range(GT)] for b in range(2)]
        ef_in = [sem(f"ef_in{b}") for b in range(2)]
        ef_whole = sem("ef_whole")
        turned_full = sem("turned_full")
        eturned_full = sem("eturned_full")
        xT_full = sem("xT_full")
        eT_full = sem("eT_full")
        hs_full = sem("hs_full")
        h_full = sem("h_full")
        dst_full = sem("dst_full")
        same_full = sem("same_full")
        prev_full = sem("prev_full")
        sum_full = sem("sum_full")
        msg_full = sem("msg_full")
        z_mul = sem("z_mul")
        z_full = sem("z_full")
        z_out = [sem(f"z_out{b}") for b in range(2)]
        stage_pe = sem("stage_pe")
        stage_dve = sem("stage_dve")
        arg_full = sem("arg_full")
        exp_full = sem("exp_full")
        x_in = [sem(f"x_in{b}") for b in range(2)]
        x_out = [sem(f"x_out{b}") for b in range(2)]
        rest_in = sem("rest_in")
        rest_out = sem("rest_out")
        var_full = sem("var_full")
        std_full = sem("std_full")
        rstd_full = sem("rstd_full")
        x_norm = sem("x_norm")
        zl_in = [sem(f"zl_in{b}") for b in range(2)]
        z_norm = sem("z_norm")
        put_ready = sem("put_ready")
        put_done = [sem(f"put_done{b}") for b in range(2)]

        x_nodes = x[0:MAIN, :].rearrange("(p r) f -> p r f", r=NR)
        out_nodes = out[0:MAIN, :].rearrange("(p r) f -> p r f", r=NR)
        x_rest = x[MAIN:N, :].rearrange("(p r) f -> p r f", r=TR)
        out_rest = out[MAIN:N, :].rearrange("(p r) f -> p r f", r=TR)
        ef_dram = edge_attr[0:(ET - 1) * P, :].rearrange("(k p) c -> p k c", p=P)
        z_tiles = z_dram.rearrange("(k p) f -> p k f", p=P)

        def window(t, offset, ap):
            return bass.AP(tensor=t.tensor, offset=offset, ap=ap)

        full = (NB - 1) * P
        odd = ET - 1 - full
        first_loads = [
            (src_rows[:, 0, :], window(src, 0, [[P, P], [1, P]])),
            (dst_rows[:, 0, :], window(dst, 0, [[P, P], [1, P + 1]])),
        ]
        index_loads = [
            (src_rows[:, 1:NB - 1, :], window(src, P * P, [[P, P], [P * P, NB - 2], [1, P]])),
            (src_rows[0:odd, NB - 1, :], window(src, full * P, [[P, odd], [1, P]])),
            (src_rows[odd:odd + 1, NB - 1, 0:LAST], window(src, (ET - 1) * P, [[LAST, 1], [1, LAST]])),
            (dst_rows[:, 1:NB - 1, :], window(dst, P * P, [[P, P], [P * P, NB - 2], [1, P + 1]])),
            (dst_rows[0:odd, NB - 1, :], window(dst, full * P, [[P, odd], [1, P + 1]])),
            (dst_rows[odd:odd + 1, NB - 1, 0:LAST], window(dst, (ET - 1) * P, [[LAST, 1], [1, LAST]])),
        ]
        hr_loads = []
        for h in range(HR):
            a, b = h * GT, (h + 1) * GT
            g = GT * P
            hr_loads += [
                (dst_hr[a:b, 1:NG - 1, :], window(dst, g - 1, [[P, GT], [g, NG - 2], [1, P + 1]])),
                (dst_hr[a:a + 1, 0, 1:P + 1], window(dst, 0, [[P, 1], [1, P]])),
                (dst_hr[a + 1:b, 0, :], window(dst, P - 1, [[P, GT - 1], [1, P + 1]])),
                (dst_hr[a:b - 1, NG - 1, :], window(dst, (NG - 1) * g - 1, [[P, GT - 1], [1, P + 1]])),
                (dst_hr[b - 1:b, NG - 1, 0:LAST + 1], window(dst, (ET - 1) * P - 1, [[LAST + 1, 1], [1, LAST + 1]])),
            ]

        def in_pairs(eng, first, last, body):
            pairs = (last - first) // 2
            with eng.Fori(0, pairs) as j:
                for u in range(2):
                    i = first + u
                    body(j * 2 + i, i % 2, j + i // 2)
            for i in range(first + 2 * pairs, last):
                body(i, i % 2, i // 2)

        block = ctx.enter_context(nc.Block())

        @block.sync
        def _(sp):
            for to, of in first_loads:
                sp.dma_start(to, of).then_inc(ld_first, 16)
            sp.wait_ge(clear_rows, 4)
            for to, of in index_loads:
                sp.dma_start(to, of).then_inc(ld_rows, 16)
            sp.dma_start(xn[1][0:TP, 0:TR, :], x_rest).then_inc(rest_in, 16)
            sp.dma_start(w_all[:, 0:D], w_node).then_inc(ld_w, 16)
            sp.dma_start(w_e[0:DE, :], w_edge).then_inc(ld_w, 16)
            sp.dma_start(w_e[DE:P, :], w_edge).then_inc(ld_w, 16)
            sp.dma_start(att[:], window(attn, 0, [[0, P], [3 * F, H], [1, 3 * F]])).then_inc(ld_w, 16)

            def load_nodes(i, par):
                sp.dma_start(xn[par][:], x_nodes[:, bass.ds(i * XR, XR), :]).then_inc(x_in[par], 16)

            def load_edges(i, par):
                sp.dma_start(ef[par][:], ef_dram[:, bass.ds(i * GT, GT), :]).then_inc(ef_in[par], 16)

            def store_z(i, par):
                sp.wait_ge(z_full, (i + 1) * GT)
                sp.dma_start(z_tiles[:, bass.ds(i * GT, GT), :], zb[par][:]).then_inc(z_out[par], 16)

            load_edges(0, 0)
            load_nodes(0, 0)
            for to, of in hr_loads:
                sp.dma_start(to, of).then_inc(ld_hr, 16)
            load_edges(1, 1)
            sp.wait_ge(rest_out, 16)
            load_nodes(1, 1)

            def ahead(i, par, uses):
                sp.wait_ge(hs_full, (i - 1) * AS)
                load_edges(i, par)
                sp.wait_ge(x_out[par], uses * 16)
                load_nodes(i, par)
                store_z(i - 2, par)

            in_pairs(sp, 2, NX, ahead)

            def load_z(q, par, uses, tiles=ZT):
                for a in range(0, tiles, GT // 2 + 1):
                    n = min(GT // 2 + 1, tiles - a)
                    sp.dma_start(xn[par][:, a:a + n, :], z_tiles[:, bass.ds(q * ZT + a, n), :]).then_inc(zl_in[par], 16)

            i = NG - 2
            sp.wait_ge(hs_full, (i - 1) * AS)
            load_edges(i, i % 2)
            sp.wait_ge(x_out[1], 16 * (NX // 2))
            sp.wait_ge(z_out[0], 16)
            sp.wait_ge(z_out[1], 16)
            load_z(0, 1, 0)
            store_z(i - 2, i % 2)
            i = NG - 1
            sp.wait_ge(hs_full, (i - 1) * AS)
            sp.dma_start(ef[0][:, 0:GT - 1, :], ef_dram[:, i * GT:ET - 1, :]).then_inc(ef_whole, 16)
            sp.wait_ge(ef_whole, 16)
            sp.dma_start(ef[0][0:LAST, GT - 1, :], edge_attr[(ET - 1) * P:E, :]).then_inc(ef_in[0], 16)
            sp.wait_ge(x_out[0], 16 * (NX // 2 + 1))
            sp.wait_ge(z_out[0], 32)
            sp.wait_ge(z_out[1], 32)
            load_z(1, 0, 0)
            store_z(i - 2, 0)
            store_z(NG - 2, 1)
            sp.wait_ge(put_done[1], 16 * ZT)
            load_z(2, 1, 1)
            store_z(NG - 1, 0)
            sp.wait_ge(z_out[0], 16 * (NG // 2 + 1))
            sp.wait_ge(z_out[1], 16 * (NG // 2))
            for q in range(3, NZ):
                par = (q + 1) % 2
                sp.wait_ge(put_done[par], 16 * ZT * ((q - 1) // 2 if par == 0 else q // 2))
                load_z(q, par, 0, min(ZT, ET - q * ZT))

        @block.gpsimd
        def _(pool):
            pool.memset(src_rows[:, NB - 1, :], 0).then_inc(clear_rows, 1)
            pool.memset(dst_rows[:, NB - 1, :], -1).then_inc(clear_rows, 1)
            pool.memset(dst_hr[:, 0, 0:1], -1).then_inc(clear_rows, 1)
            pool.memset(dst_hr[:, NG - 1, :], -1).then_inc(clear_rows, 1)
            pool.memset(ident[:], 0.0).then_inc(pool_c, 1)
            pool.memset(m_last[:], 0.0).then_inc(pool_c, 1)
            pool.wait_ge(pool_c, 2)
            nc.gpsimd.affine_select(out=ident[:], in_=ident[:], compare_op=ALU.not_equal, fill=1.0, base=0,
                                    pattern=[[-1, P]], channel_multiplier=1).then_inc(pool_id, 1)
            nc.gpsimd.affine_select(out=m_last[:], in_=m_last[:], compare_op=ALU.not_equal, fill=1.0,
                                    base=-(P - 1), pattern=[[0, 1]], channel_multiplier=1).then_inc(pool_id, 1)

            def gather(i, par, uses, again=True):
                pool.wait_ge(now_ready, i + 1)
                pool.sem_inc(pool_gate, 1)
                for t in range(GT):
                    if again:
                        pool.wait_ge(z_full, (i - 2) * GT + (t + 1))
                        pool.sem_inc(pool_gate, 1)
                    for k, rows in enumerate((xs, xd)):
                        nc.gpsimd.indirect_dma_start(
                            rows[par][:, t, :], None, x,
                            bass.IndirectOffsetOnAxis(ap=now[par][:, k, t:t + 1], axis=0)).then_inc(got[par][t], 16)

            gather(0, 0, 0, False)
            gather(1, 1, 0, False)
            in_pairs(pool, 2, NG, gather)

            pool.wait_ge(rest_out, 16)
            pool.wait_ge(x_out[0], 16 * (NX // 2 + 1))
            pool.wait_ge(x_out[1], 16 * (NX // 2))

            def scatter(q, par, tiles=ZT):
                pool.wait_ge(put_ready, q + 1)
                pool.sem_inc(pool_gate, 1)
                for t in range(tiles):
                    pool.wait_ge(z_norm, q * ZT + (t + 1))
                    pool.sem_inc(pool_gate, 1)
                    nc.gpsimd.indirect_dma_start(
                        out, bass.IndirectOffsetOnAxis(ap=put_now[par][:, t:t + 1], axis=0),
                        xn[par][:, t, :], None, bounds_check=N - 1, oob_is_err=False).then_inc(put_done[par], 16)

            in_pairs(pool, 0, NZ - 1, lambda q, par, uses: scatter(q, 1 - par))
            scatter(NZ - 1, (NX + NZ - 1) % 2, ET - (NZ - 1) * ZT)
            done = [sum(min(ZT, ET - q * ZT) for q in range(NZ) if (NX + q) % 2 == b) for b in range(2)]
            pool.wait_ge(put_done[0], 16 * done[0])
            pool.wait_ge(put_done[1], 16 * done[1])

        @block.tensor
        def _(pe):
            pe.wait_ge(pool_id, 2)
            pe.wait_ge(idx_dve, 1)
            for k in range(2):
                mm = pe.transpose(turned[1][:, k * P:(k + 1) * P], rows_f[:, k, 0, :], ident[:])
            mm.then_inc(idx_pe, 1)
            pe.wait_ge(idx_dve, 2)
            for k, bank in enumerate((stage, dst_ps, hs_ps[1])):
                for b in range(NB):
                    mm = pe.transpose(bank[:, b * P:(b + 1) * P], rows_f[:, k, b, :], ident[:])
                mm.then_inc(idx_pe, 1)
            pe.wait_ge(w_ready, 1)
            pe.matmul(sums[1][:, 0:D], zero_t[:], zero_t[:], start=True, stop=True)

            def turn_in(i, par, uses, m):
                k, b = i * AS + m, m % 2
                tiles = range(2 * m, min(2 * m + 2, GT))
                for t in tiles:
                    pe.wait_ge(got[par][t], uses * 32 + 32)
                if not isinstance(k, int) or k >= 2:
                    pe.wait_ge(xT_full, k - 1)
                for u, t in enumerate(tiles):
                    pe.transpose(turned[b][:, u * P:(u + 1) * P], xs[par][:, t, :], ident[:])
                    ins = pe.transpose(turned[b][:, (2 + u) * P:(3 + u) * P], xd[par][:, t, :], ident[:])
                ins.then_inc(turned_full, 1)

            def turn_edges(i, par, uses, m):
                k, b = i * AS + m, m % 2
                n = min(2, GT - 2 * m)
                if m == 0:
                    pe.wait_ge(ef_in[par], uses * 16 + 16)
                if not isinstance(k, int) or k >= 2:
                    pe.wait_ge(h_full, k - 1)
                    if n == 1:
                        pe.sem_inc(pe_gate, 1)
                pe.transpose(hs_ps[b][0:DE * n, 3 * P:4 * P],
                             ef[par][:, 2 * m:2 * m + n, :].rearrange("p t c -> p (t c)"),
                             ident[:]).then_inc(eturned_full, 1)

            def project(i, m):
                k, b = i * AS + m, m % 2
                n = min(2, GT - 2 * m)
                pe.wait_ge(xT_full, k + 1)
                pe.wait_ge(eT_full, k + 1)
                for u in range(n):
                    pe.matmul(hs_ps[b][:, u * HW:(u + 1) * HW], xT[b][:, u * P:(u + 1) * P], w_all[:],
                              start=(u == 0), stop=False, skip_group_check=True)
                for u in range(n):
                    pe.matmul(hs_ps[b][:, u * HW + D:(u + 1) * HW], xT[b][:, (2 + u) * P:(3 + u) * P], w_dst[:],
                              start=False, stop=False, skip_group_check=True)
                pe.matmul(hs_ps[b][:, 0:n * HW].rearrange("p (u c) -> p u c", u=n)[:, :, D:HW], eT[b][:],
                          w_edg[:, 0:n, :].rearrange("p u h -> p (u h)"), start=False, stop=True,
                          skip_group_check=True).then_inc(hs_full, 1)

            def spread_dst(i, par, t):
                k = i * GT + t
                if not isinstance(k, int) or k >= 1:
                    pe.wait_ge(same_full, k)
                pe.transpose(dst_ps[:, 0:P], dst_now[par][:, t:t + 1, 0].to_broadcast([P, P]),
                             ident[:]).then_inc(dst_full, 1)

            def add_up(i, par, t):
                k = i * GT + t
                b = (par * GT + t) % 2
                pe.wait_ge(same_full, k + 1)
                if t == 0:
                    pe.wait_ge(msg_full, i + 1)
                else:
                    pe.wait_ge(z_mul, k - 1)
                pe.matmul(sums[b][:, 0:D], same[b][:, 0, :], hb[par][:, t, 0:D], start=True, stop=False)
                pe.wait_ge(prev_full, k + 1)
                pe.matmul(sums[b][:, 0:D], same[b][:, 1, :], prev[b][:], start=False, stop=True).then_inc(sum_full, 1)

            def softmax_turn(i, q):
                pe.wait_ge(stage_dve, i * 6 + (q + 1))
                if q == 0:
                    pe.transpose(stage[0:RR, 0:P], sc[:], ident[:]).then_inc(stage_pe, 1)
                elif q == 1:
                    for c, col in enumerate((s_tmax[:, P - 1:P], s_first[:, P - 1:P], s_same[:, 0:1])):
                        mm = pe.transpose(stage[0:1, P + c * RR:P + (c + 1) * RR], col, ident[0:RR, 0:RR])
                    mm.then_inc(stage_pe, 1)
                elif q == 2:
                    pe.sem_inc(pe_gate, 1)
                    pe.transpose(stage[0:RR, 0:1], r_in2[:].rearrange("o h t -> o (h t)"),
                                 ident[0:1, 0:1]).then_inc(stage_pe, 1)
                elif q == 3:
                    pe.transpose(stage[:, 0:RR], s_exp[:], ident[0:RR, 0:RR])
                    pe.transpose(stage[:, RR:2 * RR], c_fac[:].to_broadcast([RR, P]), ident[0:RR, 0:RR])
                    pe.transpose(stage[0:1, 2 * RR:3 * RR], s_den[:, P - 1:P], ident[0:RR, 0:RR])
                    pe.transpose(stage[0:1, 3 * RR:4 * RR], c_wfac[:], ident[0:RR, 0:RR]).then_inc(stage_pe, 1)
                elif q == 4:
                    pe.sem_inc(pe_gate, 1)
                    pe.transpose(stage[0:RR, 0:1], r_din[:].rearrange("o h t -> o (h t)"),
                                 ident[0:1, 0:1]).then_inc(stage_pe, 1)
                else:
                    pe.transpose(stage[:, 0:RR], s_dtot[:], ident[0:RR, 0:RR]).then_inc(stage_pe, 1)

            def keep_busy(n):
                for _ in range(n):
                    pe.transpose(turned[0][:, 0:P], ident[:], ident[:])

            def round_(i, par, uses, edges=True, before=True, more=True):
                turns = {AS: 0, AS + 1: 1, AS + 2: 2, AS + 4: 3, AS + 5: 4, AS + 6: 5}
                for s in range(GT):
                    if edges and s + 1 < AS:
                        turn_in(i, par, uses, s + 1)
                    if before:
                        add_up(i - 1, 1 - par, s)
                        if s + 2 < GT:
                            spread_dst(i - 1, 1 - par, s + 2)
                    if edges and s + 1 < AS:
                        turn_edges(i, par, uses, s + 1)
                    if edges and s < AS:
                        project(i, s)
                    if edges and s in turns:
                        softmax_turn(i, turns[s])
                    if edges and AS <= s:
                        keep_busy(FILL)
                if edges:
                    pe.wait_ge(dst_ready, i + 1)
                    spread_dst(i, par, 0)
                if more:
                    turn_in(i + 1, 1 - par, uses + par, 0)
                    turn_edges(i + 1, 1 - par, uses + par, 0)
                if edges:
                    spread_dst(i, par, 1)

            turn_in(0, 0, 0, 0)
            turn_edges(0, 0, 0, 0)
            round_(0, 0, 0, before=False)
            in_pairs(pe, 1, NG - 1, round_)
            round_(NG - 1, 0, NG // 2, more=False)
            round_(NG, NG % 2, NG // 2, edges=False, more=False)

        @block.scalar
        def _(act):
            def std_of(n, cols, parts=P):
                act.wait_ge(var_full, n + 1)
                act.activation(st_std[0:parts, 0:cols], st_var[0:parts, 0:cols], ACT.Sqrt, scale=1.0 / D,
                               bias=eps_t[0:parts, :]).then_inc(std_full, 1)

            def norm(row, r, parts=P):
                return act.activation(row, row, ACT.Identity, scale=rstd[0:parts, r:r + 1],
                                      bias=nbias[0:parts, r:r + 1])

            std_of(0, TR, TP)
            act.wait_ge(rstd_full, 1)
            for r in range(TR):
                last = norm(xn[1][0:TP, r, :], r, TP)
            last.then_inc(x_norm, 1)
            act.wait_ge(x_norm, 1)
            act.dma_start(out_rest, xn[1][0:TP, 0:TR, :]).then_inc(rest_out, 16)

            def norm_batch(i, par, nodes, rows, first, last):
                for r in range(first, last):
                    ins = norm(xn[par][:, r, :], r)
                    if not nodes:
                        ins.then_inc(z_norm, 1)
                if nodes and last == rows:
                    ins.then_inc(x_norm, 1)
                    act.wait_ge(x_norm, i + 2)
                    act.dma_start(out_nodes[:, bass.ds(i * XR, XR), :], xn[par][:]).then_inc(x_out[par], 16)

            def copy_turned(i, m):
                k, b = i * AS + m, m % 2
                n = min(2, GT - 2 * m)
                act.wait_ge(turned_full, k + 1)
                act.activation(xT[b][:].rearrange("p (w u e) -> p w u e", w=2, u=2)[:, :, 0:n, :],
                               turned[b][:].rearrange("p (w u e) -> p w u e", w=2, u=2)[:, :, 0:n, :],
                               ACT.Copy).then_inc(xT_full, 1)
                act.wait_ge(eturned_full, k + 1)
                act.activation(eT[b][0:n * DE, :], hs_ps[b][0:n * DE, 3 * P:4 * P], ACT.Copy).then_inc(eT_full, 1)

            def copy_h(i, par, m):
                k, b = i * AS + m, m % 2
                n = min(2, GT - 2 * m)
                act.wait_ge(hs_full, k + 1)
                act.activation(hb[par][:, 2 * m:2 * m + n, :].rearrange("p t c -> p (t c)"),
                               hs_ps[b][:, 0:n * HW], ACT.Copy).then_inc(h_full, 1)

            over = 3

            def norm_part(i, par, nodes, k):
                rows, parts = (XR if nodes else ZT), GT - AS + over
                norm_batch(i, par, nodes, rows, rows * k // parts, rows * (k + 1) // parts)

            def round_(i, par, uses, edges=True, nodes=True, more=True, before=True, nodes_before=True):
                rows = XR if nodes else ZT
                for s in range(GT):
                    if edges and s < AS:
                        if s + 1 < AS:
                            copy_turned(i, s + 1)
                        copy_h(i, par, s)
                    if s == AS - 1:
                        std_of(i + 1, rows)
                    if s == AS:
                        act.wait_ge(rstd_full, i + 2)
                    if edges and s == AS + 3:
                        act.wait_ge(arg_full, i + 1)
                        act.activation(s_exp[:], s_arg[:], ACT.Exp).then_inc(exp_full, 1)
                        act.activation(c_fac[:], s_max[:, 0:1], ACT.Exp, scale=-1.0, bias=c_max[:]).then_inc(exp_full, 1)
                    if s == GT - 1 and more:
                        copy_turned(i + 1, 0)
                    if s >= AS:
                        norm_part(i, par, nodes, s - AS)
                    elif s < over and before:
                        norm_part(i - 1, 1 - par, nodes_before, GT - AS + s)

            copy_turned(0, 0)
            round_(0, 0, 0, before=False)
            in_pairs(act, 1, NX, round_)
            round_(NG - 2, 1, 0, nodes=False)
            round_(NG - 1, 0, 0, nodes=False, more=False, nodes_before=False)
            round_(NG, 1, 0, edges=False, nodes=False, more=False, nodes_before=False)
            for k in range(over):
                norm_part(NG, 1, False, GT - AS + k)
            for q in range(3, NZ):
                rows = min(ZT, ET - q * ZT)
                std_of(NX + q + 1, rows)
                act.wait_ge(rstd_full, NX + q + 2)
                norm_batch(NX + q, (NX + q) % 2, False, rows, 0, rows)

        @block.vector
        def _(dve):
            class Chain:
                base, n = 0, 0

            def link(ins):
                Chain.n += 1
                ins.then_inc(dve_c, 1)
                dve.wait_ge(dve_c, Chain.base + Chain.n)

            def fork(ins):
                Chain.n += 1
                ins.then_inc(dve_c, 1)

            def after(n):
                dve.wait_ge(dve_c, Chain.base + n)

            def nothing():
                pass

            def statistics(cols, parts=P, beside=nothing, beside2=nothing):
                s = [st[0:parts, 0:cols, q] for q in range(6)]
                a = [v[0:parts, 0:cols] for v in (st_sum, st_dif, st_m2, st_d2, st_var)]
                fork(dve.tensor_tensor(a[0], s[1], s[4], ALU.add))
                fork(dve.tensor_tensor(a[1], s[1], s[4], ALU.subtract))
                fork(dve.tensor_tensor(a[2], s[2], s[5], ALU.add))
                n = Chain.n
                beside()
                after(n)
                fork(dve.scalar_tensor_tensor(a[3], a[1], D / 4.0, a[1], ALU.mult, ALU.mult))
                n = Chain.n
                beside2()
                after(n)
                dve.tensor_tensor(a[4], a[2], a[3], ALU.add).then_inc(var_full, 1)

            def scales(n, cols, parts=P):
                dve.wait_ge(std_full, n + 1)
                link(dve.reciprocal(rstd[0:parts, 0:cols], st_std[0:parts, 0:cols]))
                dve.scalar_tensor_tensor(nbias[0:parts, 0:cols], st_sum[0:parts, 0:cols], -0.5,
                                         rstd[0:parts, 0:cols], ALU.mult, ALU.mult).then_inc(rstd_full, 1)

            fork(dve.memset(eps_t[:], EPS))
            fork(dve.memset(zero_t[:], 0.0))
            fork(dve.memset(sc[:], 0.0))
            fork(dve.memset(s_neg[:], -BIG))
            fork(dve.memset(r_mask[:], -BIG))
            fork(dve.memset(r_max[:], -BIG))
            fork(dve.memset(r_den[:], 0.0))
            fork(dve.memset(r_wfac[:], 0.0))
            fork(dve.memset(eT[0][:], 0.0))
            fork(dve.memset(eT[1][:], 0.0))
            link(dve.memset(w_edg[:], 0.0))

            dve.wait_ge(ld_first, 16 * len(first_loads))
            fork(dve.tensor_copy(rows_f[:, 0, 0, :], src_rows[:, 0, :]))
            dve.tensor_copy(rows_f[:, 1, 0, :], dst_rows[:, 0, 0:P]).then_inc(idx_dve, 1)
            dve.wait_ge(idx_pe, 1)
            for b in range(2):
                dve.tensor_copy(now[b][:], turned[1][:, 0:2 * P].rearrange("p (k t) -> p k t", k=2)
                                [:, :, b * GT:(b + 1) * GT]).then_inc(now_ready, 1)

            dve.wait_ge(ld_rows, 16 * len(index_loads))
            fork(dve.tensor_copy(rows_f[:, 0, 1:NB, :], src_rows[:, 1:NB, :]))
            fork(dve.tensor_copy(rows_f[:, 1, 1:NB, :], dst_rows[:, 1:NB, 0:P]))
            link(dve.tensor_tensor(rows_f[:, 2], dst_rows[:, :, 0:P], dst_rows[:, :, 1:P + 1], ALU.is_equal))
            dve.scalar_tensor_tensor(rows_f[:, 2], rows_f[:, 2], float(SKIP), rows_f[:, 1],
                                     ALU.mult, ALU.add).then_inc(idx_dve, 1)
            dve.wait_ge(idx_pe, 2)
            fork(dve.tensor_copy(src_col[:], stage[:]))
            dve.wait_ge(idx_pe, 3)
            fork(dve.tensor_copy(dst2[:, :, 0], dst_ps[:]))
            fork(dve.memset(dst2[:, 0:1, 1], -5.0))
            fork(dve.tensor_scalar(dst2[:, 1:ETP, 1], dst_ps[:, 0:ETP - 1], 5.0, m_last[:], ALU.add, ALU.mult))
            fork(dve.tensor_scalar(dst_col[:], dst_ps[:], 0.0, None, ALU.max))
            dve.wait_ge(idx_pe, 4)
            link(dve.tensor_copy(put_col[:], hs_ps[1][:]))
            link(dve.tensor_scalar(dst2[:, 1:ETP, 1], dst2[:, 1:ETP, 1], -5.0, None, ALU.add))

            def group_indices(i, par):
                dve.tensor_copy(now[par][:, 0, :], src_col[:, bass.ds(i * GT, GT)])
                dve.tensor_copy(now[par][:, 1, :], dst_col[:, bass.ds(i * GT, GT)]).then_inc(now_ready, 1)

            dve.wait_ge(ld_w, 64)
            for to, w, part in ((w_all[:, D:HW], w_all[:, 0:D], 0), (w_dst[:], w_all[:, 0:D], 1), (w_ea[:], w_e[:], 2)):
                link(dve.tensor_tensor(wtmp[:].rearrange("k (h f) -> k h f", h=H), w.rearrange("k (h f) -> k h f", h=H),
                                       att[:, :, part * F:(part + 1) * F], ALU.mult))
                link(dve.tensor_reduce(to, wtmp[:].rearrange("k (h f) -> k h f", h=H), AX.X, ALU.add))
            fork(dve.tensor_copy(w_edg[0:DE, 0, :], w_ea[0:DE, :]))
            link(dve.tensor_copy(w_edg[DE:P, 1, :], w_ea[DE:P, :]))
            dve.memset(prev[0][:], 0.0).then_inc(w_ready, 1)

            dve.wait_ge(rest_in, 16)
            for r in range(TR):
                ins = dve.bn_stats(st[0:TP, r, :], xn[1][0:TP, r, :])
            link(ins)
            statistics(TR, TP)
            scales(0, TR, TP)

            def runs(i):
                if isinstance(i, int) and i == 0:
                    dve.wait_ge(ld_hr, 16 * len(hr_loads))
                D_ = dst_hr[0:RR, bass.ds(i, 1), :].rearrange("r o e -> r (o e)")
                here, before = D_[:, 1:P + 1], D_[:, 0:P]
                fork(dve.tensor_tensor(s_same[:], here, before, ALU.is_equal))
                fork(dve.tensor_tensor(s_first[:], here, D_[:, 0:1].to_broadcast([RR, P]), ALU.is_equal))

            def softmax(i, par, step, beside):
                n = i * 6
                if step == -1:
                    after(Chain.n)
                    fork(dve.tensor_scalar(s_neg[:, 0:P], s_same[:], -1.0, BIG, ALU.add, ALU.mult))
                    fork(dve.tensor_scalar(s_fneg[:], s_first[:], -1.0, BIG, ALU.add, ALU.mult))
                elif step == 0:
                    dve.wait_ge(h_full, (i + 1) * AS)
                    scores = hb[par][:, :, D:D + H].rearrange("p t h -> p h t")
                    dve.scalar_tensor_tensor(sc[:, 0:H * GT].rearrange("p (h t) -> p h t", h=H), scores, NEG_SLOPE,
                                             scores, ALU.mult, ALU.max).then_inc(stage_dve, 1)
                    beside()
                elif step == 1:
                    dve.wait_ge(stage_pe, n + 1)
                    fork(dve.tensor_copy(s_lr[:], stage[0:RR, 0:P]))
                    beside()
                    after(Chain.n)
                    fork(dve.tensor_tensor_scan(s_fmax[:], s_neg[:, 0:P], s_lr[:], -BIG, ALU.add, ALU.max))
                    link(dve.tensor_copy(r_loc[:, :, 0:1], r_max[:, :, GT:GT + 1]))
                    dve.tensor_tensor_scan(s_tmax[:, ::-1], s_neg[:, 1:P + 1][:, ::-1], s_fmax[:, ::-1], -BIG,
                                           ALU.add, ALU.max).then_inc(stage_dve, 1)
                elif step == 2:
                    dve.wait_ge(stage_pe, n + 2)
                    row = [stage[0:1, P + q * RR:P + (q + 1) * RR].rearrange("o (h t) -> o h t", h=HR) for q in range(3)]
                    fork(dve.tensor_copy(r_loc[:, :, 1:GT + 1], row[0]))
                    fork(dve.tensor_scalar(r_mask[:, :, 1:GT + 1], row[1], -1.0, BIG, ALU.add, ALU.mult))
                    fork(dve.tensor_scalar(r_in[:], row[2], -1.0, BIG, ALU.add, ALU.mult))
                    after(Chain.n - 1)
                    fork(dve.tensor_tensor_scan(r_max[:].rearrange("o h t -> o (h t)"),
                                                r_mask[:].rearrange("o h t -> o (h t)"),
                                                r_loc[:].rearrange("o h t -> o (h t)"), -BIG, ALU.add, ALU.max))
                    beside()
                    after(Chain.n)
                    dve.tensor_tensor(r_in2[:], r_in[:], r_max[:, :, 0:GT], ALU.add).then_inc(stage_dve, 1)
                elif step == 3:
                    dve.wait_ge(stage_pe, n + 3)
                    fork(dve.tensor_copy(c_max[:], stage[0:RR, 0:1]))
                    beside()
                    after(Chain.n)
                    link(dve.scalar_tensor_tensor(s_max[:], s_fneg[:], c_max[:], s_tmax[:], ALU.add, ALU.max))
                    dve.tensor_tensor(s_arg[:], s_lr[:], s_max[:], ALU.subtract).then_inc(arg_full, 1)
                elif step == 4:
                    beside()
                    dve.wait_ge(exp_full, i * 2 + 2)
                    fork(dve.tensor_tensor(c_wfac[:], s_first[:, P - 1:P], c_fac[:], ALU.mult))
                    dve.tensor_tensor_scan(s_den[:], s_same[:], s_exp[:], 0.0, ALU.mult, ALU.add).then_inc(stage_dve, 1)
                    fork(dve.tensor_copy(r_dloc[:, :, 0:1], r_den[:, :, GT:GT + 1]))
                elif step == 5:
                    dve.wait_ge(stage_pe, n + 4)
                    fork(dve.tensor_copy(r_dloc[:, :, 1:GT + 1],
                                         stage[0:1, 2 * RR:3 * RR].rearrange("o (h t) -> o h t", h=HR)))
                    fork(dve.tensor_copy(r_wfac[:, :, 1:GT + 1],
                                         stage[0:1, 3 * RR:4 * RR].rearrange("o (h t) -> o h t", h=HR)))
                    fork(dve.tensor_copy(wgt[:].rearrange("p h t -> p (h t)"), stage[:, 0:RR]))
                    after(Chain.n - 1)
                    fork(dve.tensor_tensor_scan(r_den[:].rearrange("o h t -> o (h t)"),
                                                r_wfac[:].rearrange("o h t -> o (h t)"),
                                                r_dloc[:].rearrange("o h t -> o (h t)"), 0.0, ALU.mult, ALU.add))
                    fork(dve.tensor_copy(fac[par][:].rearrange("p h t -> p (h t)"), stage[:, RR:2 * RR]))
                    beside()
                    after(Chain.n)
                    dve.tensor_copy(r_din[:], r_den[:, :, 0:GT]).then_inc(stage_dve, 1)
                elif step == 6:
                    dve.wait_ge(stage_pe, n + 5)
                    fork(dve.tensor_tensor(c_den[:], stage[0:RR, 0:1], c_fac[:], ALU.mult))
                    beside()
                    after(Chain.n)
                    dve.scalar_tensor_tensor(s_dtot[:], s_first[:], c_den[:], s_den[:], ALU.mult,
                                             ALU.add).then_inc(stage_dve, 1)
                    dve.tensor_copy(dst_now[par][:], dst2[:, bass.ds(i * GT, GT), :]).then_inc(dst_ready, 1)
                    messages(par, step)
                elif step == 7:
                    dve.wait_ge(stage_pe, n + 6)
                    fork(dve.tensor_scalar(den[:].rearrange("p h t -> p (h t)"), stage[:, 0:RR], 0.5, None, ALU.max))
                    beside()
                    after(Chain.n)
                    fork(dve.tensor_tensor(rec[:], den[:, 0:H, :], den[:, H:HR, :].to_broadcast([P, H, GT]), ALU.mult))
                    messages(par, step)
                    after(Chain.n)
                    fork(dve.reciprocal(nrm[par][:], rec[:]))
                else:
                    beside()
                    messages(par, step)

            def messages(par, step):
                a, b = [GT * w // 16 for w in (0, 4, 5, 9, 13, 16)][step - 6:step - 4]
                msg = hb[par][:, a:b, 0:D].rearrange("p t (h f) -> p t h f", h=H)
                ins = dve.tensor_tensor(msg, msg, wgt[:, 0:H, a:b].rearrange("p h t -> p t h").unsqueeze(3)
                                        .to_broadcast([P, b - a, H, F]), ALU.mult)
                if b == GT:
                    ins.then_inc(msg_full, 1)

            def match(i, par, t):
                k = i * GT + t
                b = (par * GT + t) % 2
                dve.wait_ge(dst_full, k + 1)
                dve.tensor_tensor(same[b][:], dst_ps[:, 0:P].unsqueeze(1).to_broadcast([P, 2, P]),
                                  dst_now[par][:, t, :].unsqueeze(2)
                                  .to_broadcast([P, 2, P]), ALU.is_equal).then_inc(same_full, 1)

            def carry(i, par, t):
                k = i * GT + t
                b = (par * GT + t) % 2
                if not isinstance(k, int) or k >= 1:
                    dve.wait_ge(sum_full, k)
                dve.tensor_tensor(prev[b][:].rearrange("p (h f) -> p h f", h=H),
                                  sums[1 - b][:, 0:D].rearrange("p (h f) -> p h f", h=H),
                                  fac[par][:, 0:H, t:t + 1].to_broadcast([P, H, F]), ALU.mult).then_inc(prev_full, 1)

            def z_times(i, par, uses, t):
                k = i * GT + t
                b = (par * GT + t) % 2
                dve.wait_ge(sum_full, k + 1)
                if t == 0 and not (isinstance(i, int) and i < 2):
                    dve.wait_ge(z_out[par], uses * 16)
                dve.tensor_tensor(zb[par][:, t, :].rearrange("p (h f) -> p h f", h=H),
                                  sums[b][:, 0:D].rearrange("p (h f) -> p h f", h=H),
                                  nrm[par][:, :, t:t + 1].to_broadcast([P, H, F]), ALU.mult).then_inc(z_mul, 1)

            def z_plus(i, par, t):
                k = i * GT + t
                dve.wait_ge(z_mul, k + 1)
                dve.tensor_tensor(zb[par][:, t, :], zb[par][:, t, :], xd[par][:, t, :], ALU.add).then_inc(z_full, 1)

            def first_z(q, par):
                if q >= 2:
                    dve.wait_ge(put_done[par], 16 * ZT * (q // 2))
                n = min(ZT, ET - q * ZT)
                dve.tensor_copy(put_now[par][:, 0:n], put_col[:, q * ZT:q * ZT + n]).then_inc(put_ready, 1)
                parts = len(range(0, ZT, GT // 2 + 1))
                dve.wait_ge(zl_in[par], 16 * (q // 2 * parts + len(range(0, n, GT // 2 + 1))))

            def round_(i, par, uses, edges=True, before=True, nodes=True):
                q, qu = 1 - par, (uses if par else uses - 1)
                rows = XR if nodes else ZT
                for s in range(GT):
                    if before:
                        carry(i - 1, q, s)
                        if s + 1 < GT:
                            match(i - 1, q, s + 1)
                        if s:
                            z_times(i - 1, q, qu, s - 1)
                    if s == 0:
                        if nodes:
                            dve.wait_ge(x_in[par], uses * 16 + 16)
                        else:
                            first_z(i - NX, par)
                    if s < AS - 1:
                        for r in range(rows * s // (AS - 1), rows * (s + 1) // (AS - 1)):
                            ins = dve.bn_stats(st[:, r, :], xn[par][:, r, :])
                        if s == AS - 2:
                            fork(ins)
                    plus = (lambda: z_plus(i - 1, q, s - 1)) if before and s else nothing
                    if s == AS - 1:
                        after(Chain.n)
                        statistics(rows, P, (lambda: runs(i)) if edges else nothing, plus)
                    if edges and s >= AS - 1:
                        softmax(i, par, s - AS, plus)
                    if s != AS - 1 and (s < AS or not edges):
                        plus()
                    if s == AS:
                        if edges and (not isinstance(i, int) or i + 2 < NG):
                            group_indices(i + 2, par)
                        scales(i + 1, rows)
                if edges:
                    match(i, par, 0)
                if before:
                    z_times(i - 1, q, qu, GT - 1)
                    z_plus(i - 1, q, GT - 1)

            Chain.base, Chain.n = Chain.base + Chain.n, 0
            round_(0, 0, 0, before=False)
            per = Chain.n
            start = Chain.base + per

            def counted_round(i, par, uses, nodes=True):
                Chain.base, Chain.n = (i - 1) * per + start, 0
                round_(i, par, uses, nodes=nodes)
                assert Chain.n == per

            in_pairs(dve, 1, NX, counted_round)
            counted_round(NG - 2, 1, NG // 2 - 1, nodes=False)
            counted_round(NG - 1, 0, NG // 2, nodes=False)
            Chain.base, Chain.n = (NG - 1) * per + start, 0
            round_(NG, 1, NG // 2, edges=False, nodes=False)

            for q in range(3, NZ):
                par, n = (NX + q) % 2, min(ZT, ET - q * ZT)
                first_z(q, par)
                for t in range(n):
                    ins = dve.bn_stats(st[:, t, :], xn[par][:, t, :])
                link(ins)
                statistics(n)
                scales(NX + q + 1, n)


_INS = ['x', 'src', 'dst', 'edge_attr_64', 'L0_gnn_W_node', 'L0_gnn_W_edge', 'L0_gnn_attn']


def kernel(**inputs):
    import numpy as _np
    import concourse.bacc as _bacc
    from concourse import mybir as _mybir
    from concourse.bass_utils import run_bass_kernel_spmd as _run

    nc = _bacc.Bacc("TRN2", target_bir_lowering=False, num_devices=1)
    arrays, args = {}, []
    for name in _INS:
        a = _np.ascontiguousarray(inputs[name])
        arrays[f"in_{name}_dram"] = a
        args.append(nc.dram_tensor(f"in_{name}_dram", a.shape, _mybir.dt.from_np(a.dtype), kind="ExternalInput").ap())
    out = nc.dram_tensor("out_0_dram", inputs['x'].shape, _mybir.dt.float32, kind="ExternalOutput").ap()
    gnn_residual_layernorm(nc, *args, out)
    r = _run(nc, [arrays], core_ids=[0])
    return r.results[0]["out_0_dram"]
```
